# Optimizing a Trainium2 kernel written in Bass

```python
import numpy as np
import jax
import jax.numpy as jnp

def _softmax(x, axis=-1):
    return jax.nn.softmax(x, axis=axis)

def _gelu(x):
    return jax.nn.gelu(x, approximate=True)

def _silu(x):
    return jax.nn.silu(x)

def _sigmoid(x):
    return jax.nn.sigmoid(x)

def _layernorm(x, axis=-1, eps=1e-05):
    m = jnp.mean(x, axis=axis, keepdims=True)
    v = jnp.var(x, axis=axis, keepdims=True)
    return (x - m) / jnp.sqrt(v + eps)

def _scatter_add(tgt, idx, src, axis=0):
    return tgt.at[idx].add(src)

def _segment_sum(src, seg, n):
    return jax.ops.segment_sum(src, seg, n)
kernel_name = 'mk_rec_standalone_d1_rec_r8_47949d'

def setup_inputs(seed: int=0):
    np.random.seed(seed)
    _w = jnp.asarray

    def _rec_inputs():
        import jax
        import jax.numpy as jnp
        _rk = jax.random.key(seed)
        r_x = jax.random.uniform(jax.random.fold_in(_rk, 1), (1024, 10240), jnp.float32, 0.0, 1)
        return r_x
    r_x = _rec_inputs()

    def _L0_rec_setup():
        import jax, jax.numpy as jnp
        import numpy as np
        F = 5120

        def leaky_relu(x):
            return jnp.maximum(0.05 * x, x)

        def layer_norm(x):
            mu = jnp.mean(x, axis=-1, keepdims=True)
            sigma = jnp.sqrt(jnp.mean((x - mu) ** 2, axis=-1, keepdims=True))
            return (x - mu) / sigma
        key = jax.random.key(seed)
        k_x, k1, k2, k3, k4 = jax.random.split(key, 5)
        B = 256
        x = jax.random.uniform(k_x, (B, 2 * F), dtype=jnp.float32)
        W1 = jax.random.normal(k1, (256, F), dtype=jnp.float32) * 0.01
        W2 = jax.random.normal(k2, (64, 256), dtype=jnp.float32) * 0.05
        W3 = jax.random.normal(k3, (8, 128), dtype=jnp.float32) * 0.1
        W4 = jax.random.normal(k4, (1, 8), dtype=jnp.float32) * 0.3
        return {'x': x, 'W1': W1, 'W2': W2, 'W3': W3, 'W4': W4}
    _L0_rec_all = _L0_rec_setup()
    _L0_rec_in = {k: v for k, v in _L0_rec_all.items() if k in ('W1', 'W2', 'W3', 'W4')}
    del _L0_rec_all
    return {'r_x': r_x, 'L0_rec_W1': _L0_rec_in['W1'], 'L0_rec_W2': _L0_rec_in['W2'], 'L0_rec_W3': _L0_rec_in['W3'], 'L0_rec_W4': _L0_rec_in['W4']}

def reference(r_x, L0_rec_W1, L0_rec_W2, L0_rec_W3, L0_rec_W4):
    import jax
    import jax.numpy as jnp

    def _L0_rec_ref(x, W1, W2, W3, W4):
        import jax, jax.numpy as jnp
        import numpy as np
        F = 5120

        def leaky_relu(x):
            return jnp.maximum(0.05 * x, x)

        def layer_norm(x):
            mu = jnp.mean(x, axis=-1, keepdims=True)
            sigma = jnp.sqrt(jnp.mean((x - mu) ** 2, axis=-1, keepdims=True))
            return (x - mu) / sigma
        x = x.reshape(-1, 2 * F)
        x1, x2 = (x[:, :F], x[:, F:])
        h1 = leaky_relu(layer_norm(x1 @ W1.T))
        h2 = leaky_relu(layer_norm(x2 @ W1.T))
        h1 = leaky_relu(layer_norm(h1 @ W2.T))
        h2 = leaky_relu(layer_norm(h2 @ W2.T))
        h = jnp.concatenate([h1, h2], axis=-1)
        h = leaky_relu(layer_norm(h @ W3.T))
        return h @ W4.T
    y = _L0_rec_ref(r_x, L0_rec_W1, L0_rec_W2, L0_rec_W3, L0_rec_W4)
    return y

_drawn_inputs = setup_inputs


def setup_inputs(seed=0):
    import zlib

    import numpy as np

    out = dict(_drawn_inputs(seed))
    spreads = {}
    factors = {}
    for name, (base, spread) in spreads.items():
        noise = np.random.default_rng([zlib.crc32(name.encode()), seed]).standard_normal(out[name].shape)
        drawn = base * np.exp(spread * noise) if base else spread * noise
        out[name] = jnp.asarray(drawn.astype(out[name].dtype))
    for name, factor in factors.items():
        out[name] = (out[name] * factor).astype(out[name].dtype)
    return out
```

```python
from contextlib import ExitStack

import concourse.bass as bass
from concourse import mybir

ALU = mybir.AluOpType
ACT = mybir.ActivationFunctionType
AX = mybir.AxisListType
F32 = mybir.dt.float32
F32R = mybir.dt.float32r

P = 128
F = 5120
N1, N2, N3 = 256, 64, 8
ROWS = 1024
CHUNKS = F // P
UC = 2
UNITS = CHUNKS // UC
RING = 4
ROUNDS = UNITS // RING
GR = 256
GROUPS = ROWS // GR
T = GR // P
GC = 2 * GR
TILES = ROWS // P
M = N1 // P
J = 2 * T
LEAK = 0.05
EPI = 12


def rec_kernel(nc, x, w1, w2, w3, w4, out):
    with ExitStack() as ctx:
        def sb(name, shape, dt=F32):
            return ctx.enter_context(nc.sbuf_tensor(name, shape, dt))

        def ps(name, shape):
            return ctx.enter_context(nc.psum_tensor(name, shape, F32))

        def sem(name):
            return ctx.enter_context(nc.semaphore(name))

        x_raw = sb("x_raw", [P, RING, UC * GC])
        x_hi = sb("x_hi", [P, RING, UC * GC], F32R)
        x_lo = sb("x_lo", [P, RING, UC * GC], F32R)
        w_raw = sb("w_raw", [P, UNITS, UC * N1])
        w_hi = sb("w_hi", [P, RING, UC * N1], F32R)
        w_lo = sb("w_lo", [P, RING, UC * N1], F32R)
        w2_sb = sb("w2_sb", [P, M, N2])
        w3_sb = sb("w3_sb", [P, N3])
        w4_sb = sb("w4_sb", [P, T, N3])
        ident = sb("ident", [P, P])
        h1_fm = sb("h1_fm", [P, M, GC])
        a1 = sb("a1", [P, J, N1])
        a1_fm = sb("a1_fm", [P, M, GC])
        a2 = sb("a2", [P, T, 2 * N2])
        a2_fm = sb("a2_fm", [P, T, P])
        a3 = sb("a3", [P, T, N3])
        prod = sb("prod", [P, T, N3])
        y = sb("y", [P, TILES])
        stats = sb("stats", [P, J, 6])
        mean2 = sb("mean2", [P, J])
        dev = sb("dev", [P, J])
        gap = sb("gap", [P, J])
        var = sb("var", [P, J])
        sigma = sb("sigma", [P, J])
        inv0 = sb("inv0", [P, J])
        corr = sb("corr", [P, J])
        inv = sb("inv", [P, J])
        shift = sb("shift", [P, J])

        acc = ps("acc", [P, 2, M, GC])
        rows_ps = ps("rows_ps", [P, J, N1])
        feat_ps = ps("feat_ps", [P, M, GC])

        l2_sums = rows_ps[:, 0, :].rearrange("p (j n) -> p j n", j=J)
        l3_sums = rows_ps[:, 2, 0:T * N3].rearrange("p (t n) -> p t n", t=T)
        a2_blocks = a2[:, :, :].rearrange("p t (h n) -> p (t h) n", h=2)

        sums = [rows_ps, l2_sums, l3_sums]
        normed = [a1, a2_blocks, a3]

        x_landed = [sem(f"x_landed{s}") for s in range(RING)]
        w_landed = [sem(f"w_landed{s}") for s in range(RING)]
        small_landed = sem("small_landed")
        ident_zero = sem("ident_zero")
        ident_ready = sem("ident_ready")
        hi_ready = sem("hi_ready")
        lo_ready = sem("lo_ready")
        multiplied = sem("multiplied")
        h1_copied = sem("h1_copied")
        rows_turned = sem("rows_turned")
        stat_step = sem("stat_step")
        var_ready = sem("var_ready")
        sigma_ready = sem("sigma_ready")
        norm_ready = sem("norm_ready")
        a1_turned = sem("a1_turned")
        a1_copied = sem("a1_copied")
        layer2_done = sem("layer2_done")
        a2_turned = sem("a2_turned")
        a2_copied = sem("a2_copied")
        layer3_done = sem("layer3_done")
        scaled = [sem(f"scaled{k + 1}") for k in range(3)]
        activated = [sem(f"activated{k + 1}") for k in range(3)]
        prod_ready = sem("prod_ready")
        y_ready = sem("y_ready")
        y_stored = sem("y_stored")

        block = ctx.enter_context(nc.Block())

        NORM_BLOCKS = [J, J, T]
        WIDTHS = [N1, N2, N3]
        NORM_STEPS = [7 for _ in NORM_BLOCKS]

        @block.sync
        def _(sp):
            def load(g, r, s, first):
                u = r * RING + s
                if not first:
                    sp.wait_ge(lo_ready, g * UNITS + (r - 1) * RING + s + 1)
                if g is 0:
                    sp.dma_start(w_raw[:, bass.ds(u, 1), :], w1[bass.ds(u, 1)].rearrange("a p n -> p a n")).then_inc(w_landed[s], 16)
                sp.dma_start(x_raw[:, s, :], x[g, bass.ds(u, 1)].rearrange("a p n -> p (a n)")).then_inc(x_landed[s], 16)

            for s in range(RING):
                load(0, 0, s, True)
            sp.dma_start(w2_sb[:], w2).then_inc(small_landed, 16)
            sp.dma_start(w3_sb[:], w3).then_inc(small_landed, 16)
            sp.dma_start(w4_sb[:], w4.rearrange("(o t) n -> o t n", o=1).broadcast_to([P, T, N3])).then_inc(small_landed, 16)
            with sp.Fori(1, ROUNDS) as r:
                for s in range(RING):
                    load(0, r, s, False)
            with sp.Fori(1, GROUPS) as g:
                with sp.Fori(0, ROUNDS) as r:
                    for s in range(RING):
                        load(g, r, s, False)
            sp.wait_ge(y_ready, GROUPS)
            sp.dma_start(out, y[:]).then_inc(y_stored, 16)
            sp.wait_ge(y_stored, 16)

        @block.gpsimd
        def _(pool):
            pool.memset(ident[:], 0.0).then_inc(ident_zero, 1)
            pool.wait_ge(ident_zero, 1)
            pool.affine_select(out=ident[:], in_=ident[:], compare_op=ALU.not_equal, fill=1.0,
                               base=0, pattern=[[-1, P]], channel_multiplier=1).then_inc(ident_ready, 1)

        @block.scalar
        def _(act):
            def split_hi(g, r, s, first=False):
                u = r * RING + s
                act.wait_ge(w_landed[s], 16 * (r + 1) if g is 0 else 16 * ROUNDS)
                if not first:
                    act.wait_ge(multiplied, g * UNITS + (r - 1) * RING + s + 1)
                act.copy(w_hi[:, s, :], w_raw[:, u, :])
                act.wait_ge(x_landed[s], 16 * (g * ROUNDS + r + 1))
                act.copy(x_hi[:, s, :], x_raw[:, s, :]).then_inc(hi_ready, 1)

            def copy_h1(e):
                act.wait_ge(multiplied, (e + 1) * UNITS)
                act.copy(h1_fm[:, 0, :], acc[:, e % 2, 0, :]).then_inc(h1_copied, 1)

            def root(e, layer):
                n = NORM_BLOCKS[layer]
                act.wait_ge(var_ready, 3 * e + layer + 1)
                act.activation(sigma[:, 0:n], var[:, 0:n], ACT.Sqrt).then_inc(sigma_ready, 1)

            def scale_blocks(e, layer):
                act.wait_ge(norm_ready, 3 * e + layer + 1)
                for j in range(NORM_BLOCKS[layer]):
                    act.activation(normed[layer][:, j, :], sums[layer][:, j, :], ACT.Identity,
                                   bias=shift[:, j:j + 1], scale=inv[:, j:j + 1]).then_inc(scaled[layer], 1)

            def copy_a1(e):
                act.wait_ge(a1_turned, e + 1)
                act.copy(a1_fm[:, 0, :], feat_ps[:, 0, :]).then_inc(a1_copied, 1)

            def stages(e, n):
                if n == 2:
                    copy_h1(e)
                if n == 4:
                    root(e, 0)
                    scale_blocks(e, 0)
                if n == 6:
                    copy_a1(e)
                if n == 7:
                    root(e, 1)
                    scale_blocks(e, 1)
                if n == 10:
                    root(e, 2)
                    scale_blocks(e, 2)

            for s in range(RING):
                split_hi(0, 0, s, True)
            with act.Fori(1, ROUNDS) as r:
                for s in range(RING):
                    split_hi(0, r, s)
            with act.Fori(1, GROUPS) as g:
                for n in range(EPI):
                    split_hi(g, n // RING, n % RING)
                    stages(g - 1, n)
                with act.Fori(EPI // RING, ROUNDS) as r:
                    for s in range(RING):
                        split_hi(g, r, s)
            for n in range(EPI):
                stages(GROUPS - 1, n)

        @block.vector
        def _(dve):
            def split_lo(g, r, s, first=False):
                u = r * RING + s
                dve.wait_ge(hi_ready, g * UNITS + u + 1)
                dve.tensor_tensor(w_lo[:, s, :], w_raw[:, u, :], w_hi[:, s, :].bitcast(F32), ALU.subtract)
                dve.tensor_tensor(x_lo[:, s, :], x_raw[:, s, :], x_hi[:, s, :].bitcast(F32),
                                  ALU.subtract).then_inc(lo_ready, 1)

            def copy_h1(e):
                dve.wait_ge(multiplied, (e + 1) * UNITS)
                dve.tensor_copy(h1_fm[:, 1, :], acc[:, e % 2, 1, :]).then_inc(h1_copied, 1)

            def normalise(e, layer, src_sem):
                n = NORM_BLOCKS[layer]
                at = [e * sum(NORM_STEPS) + sum(NORM_STEPS[:layer])]

                def step(ins):
                    at[0] = at[0] + 1
                    ins.then_inc(stat_step, 1)
                    return at[0]

                dve.wait_ge(src_sem, e + 1)
                for j in range(n):
                    ins = dve.bn_stats(stats[:, j, :], sums[layer][:, j, :])
                dve.wait_ge(stat_step, step(ins))
                mean_e, dev_e, mean_o, dev_o = [stats[:, 0:n, k] for k in (1, 2, 4, 5)]
                dve.tensor_tensor(mean2[:, 0:n], mean_e, mean_o, ALU.add)
                dve.tensor_tensor(dev[:, 0:n], dev_e, dev_o, ALU.add)
                dve.wait_ge(stat_step, step(dve.tensor_tensor(gap[:, 0:n], mean_e, mean_o, ALU.subtract)))
                dve.wait_ge(stat_step, step(dve.scalar_tensor_tensor(
                    out=gap[:, 0:n], in0=gap[:, 0:n], scalar=0.25, in1=gap[:, 0:n],
                    op0=ALU.mult, op1=ALU.mult)))
                dve.scalar_tensor_tensor(out=var[:, 0:n], in0=dev[:, 0:n], scalar=1.0 / WIDTHS[layer],
                                         in1=gap[:, 0:n], op0=ALU.mult, op1=ALU.add).then_inc(var_ready, 1)
                dve.wait_ge(sigma_ready, 3 * e + layer + 1)
                dve.wait_ge(stat_step, step(dve.reciprocal(inv0[:, 0:n], sigma[:, 0:n])))
                dve.wait_ge(stat_step, step(dve.scalar_tensor_tensor(
                    out=corr[:, 0:n], in0=inv0[:, 0:n], scalar=-0.5, in1=inv0[:, 0:n],
                    op0=ALU.mult, op1=ALU.mult)))
                dve.wait_ge(stat_step, step(dve.tensor_tensor(
                    corr[:, 0:n], corr[:, 0:n], var[:, 0:n], ALU.mult)))
                dve.wait_ge(stat_step, step(dve.scalar_tensor_tensor(
                    out=inv[:, 0:n], in0=corr[:, 0:n], scalar=1.5, in1=inv0[:, 0:n],
                    op0=ALU.add, op1=ALU.mult)))
                ins = dve.scalar_tensor_tensor(out=shift[:, 0:n], in0=mean2[:, 0:n], scalar=-0.5,
                                               in1=inv[:, 0:n], op0=ALU.mult, op1=ALU.mult)
                ins.then_inc(norm_ready, 1)

            def copy_a1(e):
                dve.wait_ge(a1_turned, e + 1)
                dve.tensor_copy(a1_fm[:, 1, :], feat_ps[:, 1, :]).then_inc(a1_copied, 1)

            def copy_a2(e):
                dve.wait_ge(a2_turned, e + 1)
                dve.tensor_copy(a2_fm[:, :, :], feat_ps[:, 0, 0:T * P].rearrange("p (t n) -> p t n", t=T))\
                    .then_inc(a2_copied, 1)

            def leak(e, layer):
                n = NORM_BLOCKS[layer]
                for j in range(n):
                    dve.wait_ge(scaled[layer], n * e + j + 1)
                    h = normed[layer][:, j, :]
                    dve.scalar_tensor_tensor(out=h, in0=h, scalar=LEAK, in1=h, op0=ALU.mult,
                                             op1=ALU.max).then_inc(activated[layer], 1)

            def last_layer(e):
                dve.wait_ge(activated[2], T * (e + 1))
                dve.tensor_tensor(prod[:], a3[:], w4_sb[:], ALU.mult).then_inc(prod_ready, 1)
                dve.wait_ge(prod_ready, e + 1)
                dve.tensor_reduce(y[:, bass.ds(e * T, T)], prod[:], AX.X, ALU.add).then_inc(y_ready, 1)

            def stages(e, n):
                if n == 2:
                    copy_h1(e)
                if n == 3:
                    normalise(e, 0, rows_turned)
                if n == 4:
                    leak(e, 0)
                if n == 6:
                    copy_a1(e)
                if n == 7:
                    normalise(e, 1, layer2_done)
                    leak(e, 1)
                if n == 9:
                    copy_a2(e)
                if n == 10:
                    normalise(e, 2, layer3_done)
                    leak(e, 2)
                if n == 11:
                    last_layer(e)

            dve.wait_ge(small_landed, 48)
            with dve.Fori(0, ROUNDS) as r:
                for s in range(RING):
                    split_lo(0, r, s)
            with dve.Fori(1, GROUPS) as g:
                for n in range(EPI):
                    split_lo(g, n // RING, n % RING)
                    stages(g - 1, n)
                with dve.Fori(EPI // RING, ROUNDS) as r:
                    for s in range(RING):
                        split_lo(g, r, s)
            for n in range(EPI):
                stages(GROUPS - 1, n)

        @block.tensor
        def _(pe):
            def multiply(g, r, s, start=False):
                wh = w_hi[:, s, :].rearrange("p (c m n) -> p c m n", c=UC, m=M)
                wl = w_lo[:, s, :].rearrange("p (c m n) -> p c m n", c=UC, m=M)
                xh = x_hi[:, s, :].rearrange("p (c n) -> p c n", c=UC)
                xl = x_lo[:, s, :].rearrange("p (c n) -> p c n", c=UC)
                pe.wait_ge(hi_ready, g * UNITS + r * RING + s + 1)
                for c in range(UC):
                    for m in range(M):
                        pe.matmul(acc[:, g % 2, m, :], wh[:, c, m, :], xh[:, c, :],
                                  start=(start and c == 0), stop=False, skip_group_check=True)
                pe.wait_ge(lo_ready, g * UNITS + r * RING + s + 1)
                for c in range(UC):
                    for m in range(M):
                        pe.matmul(acc[:, g % 2, m, :], wh[:, c, m, :], xl[:, c, :],
                                  start=False, stop=False, skip_group_check=True)
                        ins = pe.matmul(acc[:, g % 2, m, :], wl[:, c, m, :], xh[:, c, :],
                                        start=False, stop=True, skip_group_check=True)
                ins.then_inc(multiplied, 1)

            def turn_h1(e):
                pe.wait_ge(h1_copied, 2 * (e + 1))
                for j in range(J):
                    for m in range(M):
                        ins = pe.transpose(rows_ps[:, j, m * P:(m + 1) * P], h1_fm[:, m, j * P:(j + 1) * P], ident[:])
                ins.then_inc(rows_turned, 1)

            def turn_a1(e):
                for j in range(J):
                    pe.wait_ge(activated[0], J * e + j + 1)
                    for m in range(M):
                        ins = pe.transpose(feat_ps[:, m, j * P:(j + 1) * P], a1[:, j, m * P:(m + 1) * P], ident[:])
                ins.then_inc(a1_turned, 1)

            def layer2(e):
                pe.wait_ge(a1_copied, 2 * (e + 1))
                for j in range(J):
                    h, t = j // T, j % T
                    for m in range(M):
                        ins = pe.matmul(l2_sums[:, t * 2 + h, :], a1_fm[:, m, j * P:(j + 1) * P], w2_sb[:, m, :],
                                        start=(m == 0), stop=(m == M - 1))
                ins.then_inc(layer2_done, 1)

            def turn_a2(e):
                for t in range(T):
                    pe.wait_ge(activated[1], J * e + 2 * (t + 1))
                    ins = pe.transpose(feat_ps[:, 0, t * P:(t + 1) * P], a2[:, t, :], ident[:])
                ins.then_inc(a2_turned, 1)

            def layer3(e):
                pe.wait_ge(a2_copied, e + 1)
                for t in range(T):
                    ins = pe.matmul(l3_sums[:, t, :], a2_fm[:, t, :], w3_sb[:], start=True, stop=True)
                ins.then_inc(layer3_done, 1)

            def stages(e, n):
                if n == 0:
                    turn_h1(e)
                if n == 3:
                    turn_a1(e)
                if n == 4:
                    layer2(e)
                if n == 7:
                    turn_a2(e)
                if n == 8:
                    layer3(e)

            for s in range(RING):
                multiply(0, 0, s, start=(s == 0))
            pe.wait_ge(ident_ready, 1)
            pe.wait_ge(small_landed, 48)
            with pe.Fori(1, ROUNDS) as r:
                for s in range(RING):
                    multiply(0, r, s)
            with pe.Fori(1, GROUPS) as g:
                for n in range(EPI):
                    multiply(g, n // RING, n % RING, start=(n == 0))
                    stages(g - 1, n)
                with pe.Fori(EPI // RING, ROUNDS) as r:
                    for s in range(RING):
                        multiply(g, r, s)
            for n in range(EPI):
                stages(GROUPS - 1, n)


def kernel(r_x, L0_rec_W1, L0_rec_W2, L0_rec_W3, L0_rec_W4):
    import numpy as np
    import concourse.bacc as bacc
    from concourse.bass_utils import run_bass_kernel_spmd

    x = np.asarray(r_x).reshape(P, GROUPS, T, 2, UNITS, UC, P)
    x = np.ascontiguousarray(x.transpose(1, 4, 6, 5, 3, 2, 0)).reshape(GROUPS, UNITS, P, UC * GC)
    w1 = np.asarray(L0_rec_W1).reshape(N1, UNITS, UC, P)
    w1 = np.ascontiguousarray(w1.transpose(1, 3, 2, 0)).reshape(UNITS, P, UC * N1)
    w2 = np.ascontiguousarray(np.asarray(L0_rec_W2).reshape(N2, M, P).transpose(2, 1, 0))
    w3 = np.ascontiguousarray(np.asarray(L0_rec_W3).T)
    w4 = np.ascontiguousarray(np.concatenate([np.asarray(L0_rec_W4)] * T))

    nc = bacc.Bacc("TRN2", target_bir_lowering=False, num_devices=1)
    arrays = {"x": x, "w1": w1, "w2": w2, "w3": w3, "w4": w4}
    args = [nc.dram_tensor(n, a.shape, mybir.dt.from_np(a.dtype), kind="ExternalInput").ap() for n, a in arrays.items()]
    out = nc.dram_tensor("out", (P, TILES), F32, kind="ExternalOutput").ap()
    rec_kernel(nc, *args, out)
    r = run_bass_kernel_spmd(nc, [arrays], core_ids=[0])
    return np.asarray(r.results[0]["out"]).reshape(ROWS, 1)
```

```python
from contextlib import ExitStack

import concourse.bass as bass
from concourse import mybir

ALU = mybir.AluOpType
ACT = mybir.ActivationFunctionType
AX = mybir.AxisListType
F32 = mybir.dt.float32
F32R = mybir.dt.float32r

P = 128
F = 5120
N1, N2, N3 = 256, 64, 8
ROWS = 1024
CHUNKS = F // P
UC = 2
UNITS = CHUNKS // UC
RING = 4
ROUNDS = UNITS // RING
GR = 256
GROUPS = ROWS // GR
T = GR // P
GC = 2 * GR
TILES = ROWS // P
M = N1 // P
J = 2 * T
LEAK = 0.05
EPI = 12


def rec_kernel(nc, x, w1, w2, w3, w4, out):
    with ExitStack() as ctx:
        def sb(name, shape, dt=F32):
            return ctx.enter_context(nc.sbuf_tensor(name, shape, dt))

        def ps(name, shape):
            return ctx.enter_context(nc.psum_tensor(name, shape, F32))

        def sem(name):
            return ctx.enter_context(nc.semaphore(name))

        x_raw = sb("x_raw", [P, RING, UC * GC])
        x_hi = sb("x_hi", [P, RING, UC * GC], F32R)
        x_lo = sb("x_lo", [P, RING, UC * GC], F32R)
        w_raw = sb("w_raw", [P, UNITS, UC * N1])
        w_hi = sb("w_hi", [P, RING, UC * N1], F32R)
        w_lo = sb("w_lo", [P, RING, UC * N1], F32R)
        w2_sb = sb("w2_sb", [P, M, N2])
        w3_sb = sb("w3_sb", [P, 2 * N3])
        w4_sb = sb("w4_sb", [P, T, N3])
        ident = sb("ident", [P, P])
        h1_fm = sb("h1_fm", [P, M, GC])
        a1 = sb("a1", [P, J, N1])
        a1_fm = sb("a1_fm", [P, M, GC])
        h2 = sb("h2", [P, J, N2])
        a2 = sb("a2", [P, J, N2])
        a2_fm = sb("a2_fm", [P, T, P])
        h3 = sb("h3", [P, T, N3])
        a3 = sb("a3", [P, T, N3])
        weighted = sb("weighted", [P, T, N3])
        y_sum = sb("y_sum", [P, T])
        y = sb("y", [P, TILES])
        stats = [sb(f"stats{k}", [P, n, 6]) for k, n in enumerate((J, J, T), 1)]
        neg_mean = [sb(f"neg_mean{k}", [P, n]) for k, n in enumerate((J, J, T), 1)]
        dev = [sb(f"dev{k}", [P, n]) for k, n in enumerate((J, J, T), 1)]
        gap = [sb(f"gap{k}", [P, n]) for k, n in enumerate((J, J, T), 1)]
        var = [sb(f"var{k}", [P, n]) for k, n in enumerate((J, J, T), 1)]
        inv = [sb(f"inv{k}", [P, n]) for k, n in enumerate((J, J, T), 1)]
        minus_half = sb("minus_half", [P, J])

        acc = ps("acc", [P, 2, M, GC])
        rows_ps = ps("rows_ps", [P, T, 2 * N1])
        feat_ps = ps("feat_ps", [P, T, M * 2 * P])

        h1_ps = rows_ps[:, :, :].rearrange("p t (h n) -> p t h n", h=2)
        h2_ps = rows_ps[:, :, 0:2 * N2].rearrange("p t (h n) -> p t h n", h=2)
        h3_ps = rows_ps[:, :, 2 * N2:2 * N2 + 2 * N3].rearrange("p t (h n) -> p t h n", h=2)
        a1_ps = feat_ps[:, :, :].rearrange("p t (m n) -> p t m n", m=M)
        a2_ps = feat_ps[:, :, 0:P]

        x_landed = [sem(f"x_landed{s}") for s in range(RING)]
        w_landed = [sem(f"w_landed{s}") for s in range(RING)]
        first_w_landed = sem("first_w_landed")
        first_x_landed = sem("first_x_landed")
        small_landed = sem("small_landed")
        ident_zero = sem("ident_zero")
        ident_ready = sem("ident_ready")
        half_ready = sem("half_ready")
        first_hi = sem("first_hi")
        first_lo = sem("first_lo")
        hi_ready = sem("hi_ready")
        lo_ready = sem("lo_ready")
        multiplied = sem("multiplied")
        h1_copied = [sem(f"h1_copied{t}") for t in range(T)]
        a1_copied = [sem(f"a1_copied{t}") for t in range(T)]
        h1_turned = sem("h1_turned")
        mean1_ready = sem("mean1_ready")
        centred1 = sem("centred1")
        a1_ready = sem("a1_ready")
        a1_turned = sem("a1_turned")
        h2_summed = sem("h2_summed")
        h2_scaled = sem("h2_scaled")
        a2_ready = sem("a2_ready")
        a2_turned = sem("a2_turned")
        a2_copied = sem("a2_copied")
        h3_summed = sem("h3_summed")
        var_ready = [sem(f"var{k}_ready") for k in (1, 2, 3)]
        inv_ready = [sem(f"inv{k}_ready") for k in (1, 2, 3)]
        y_ready = sem("y_ready")
        dve_step = sem("dve_step")
        y_stored = sem("y_stored")

        block = ctx.enter_context(nc.Block())

        @block.sync
        def _(sp):
            def load(g, r, s, first=False):
                u = r * RING + s
                if not first:
                    sp.wait_ge(lo_ready, g * UNITS + (r - 1) * RING + s + 1)
                if g is 0:
                    sp.dma_start(w_raw[:, bass.ds(u, 1), :],
                                 w1[bass.ds(u, 1)].rearrange("a p n -> p a n")).then_inc(w_landed[s], 16)
                sp.dma_start(x_raw[:, s, :],
                             x[g, bass.ds(u, 1)].rearrange("a p n -> p (a n)")).then_inc(x_landed[s], 16)

            sp.dma_start(w_raw[:, 0, 0:N1], w1[0, :, 0:N1]).then_inc(first_w_landed, 16)
            sp.dma_start(x_raw[:, 0, 0:GC], x[0, 0, :, 0:GC]).then_inc(first_x_landed, 16)
            sp.dma_start(w_raw[:, 0, N1:], w1[0, :, N1:]).then_inc(w_landed[0], 16)
            sp.dma_start(x_raw[:, 0, GC:], x[0, 0, :, GC:]).then_inc(x_landed[0], 16)
            for s in range(1, RING):
                load(0, 0, s, first=True)
            with sp.Fori(1, ROUNDS) as r:
                for s in range(RING):
                    load(0, r, s)
            sp.dma_start(w2_sb[:], w2).then_inc(small_landed, 16)
            sp.dma_start(w3_sb[:], w3).then_inc(small_landed, 16)
            sp.dma_start(w4_sb[:], w4.rearrange("(o t) n -> o t n", o=1).broadcast_to([P, T, N3]))\
                .then_inc(small_landed, 16)
            with sp.Fori(1, GROUPS) as g:
                with sp.Fori(0, ROUNDS) as r:
                    for s in range(RING):
                        load(g, r, s)
            sp.wait_ge(y_ready, GROUPS)
            sp.dma_start(out, y[:]).then_inc(y_stored, 16)
            sp.wait_ge(y_stored, 16)

        @block.gpsimd
        def _(pool):
            pool.memset(ident[:], 0.0).then_inc(ident_zero, 1)
            pool.memset(minus_half[:], -0.5).then_inc(half_ready, 1)
            pool.wait_ge(ident_zero, 1)
            pool.affine_select(out=ident[:], in_=ident[:], compare_op=ALU.not_equal, fill=1.0,
                               base=0, pattern=[[-1, P]], channel_multiplier=1).then_inc(ident_ready, 1)
            pool.wait_ge(half_ready, 1)

            def invert(e, layer):
                n = (J, J, T)[layer]
                pool.wait_ge(var_ready[layer], e + 1)
                pool.tensor_tensor(inv[layer][:], var[layer][:], minus_half[:, 0:n], ALU.pow)\
                    .then_inc(inv_ready[layer], 1)

            with pool.Fori(0, GROUPS) as e:
                for layer in range(3):
                    invert(e, layer)

        @block.scalar
        def _(act):
            def split_hi(g, r, s):
                u = r * RING + s
                act.wait_ge(w_landed[s], 16 * (r + 1) if g is 0 else 16 * ROUNDS)
                if not (g is 0 and r is 0):
                    act.wait_ge(multiplied, g * UNITS + (r - 1) * RING + s + 1)
                act.copy(w_hi[:, s, :], w_raw[:, u, :])
                act.wait_ge(x_landed[s], 16 * (g * ROUNDS + r + 1))
                act.copy(x_hi[:, s, :], x_raw[:, s, :]).then_inc(hi_ready, 1)

            def copy_h1(e):
                act.wait_ge(multiplied, (e + 1) * UNITS)
                for t in range(T):
                    cols = slice(t * 2 * P, (t + 1) * 2 * P)
                    act.copy(h1_fm[:, 0, cols], acc[:, e % 2, 0, cols]).then_inc(h1_copied[t], 1)

            def centre1(e):
                for t in range(T):
                    act.wait_ge(mean1_ready, T * e + t + 1)
                    for h in range(2):
                        j = 2 * t + h
                        ins = act.activation(a1[:, j, :], h1_ps[:, t, h, :], ACT.Identity,
                                             bias=neg_mean[0][:, j:j + 1], scale=2.0)
                    ins.then_inc(centred1, 1)

            def copy_a1(e):
                act.wait_ge(a1_turned, T * e + 1)
                act.copy(a1_fm[:, :, 0:2 * P], a1_ps[:, 0]).then_inc(a1_copied[0], 1)

            def scale_h2(e):
                act.wait_ge(inv_ready[0], e + 1)
                for t in range(T):
                    act.wait_ge(h2_summed, T * e + t + 1)
                    for h in range(2):
                        j = 2 * t + h
                        ins = act.activation(h2[:, j, :], h2_ps[:, t, h, :], ACT.Copy, scale=inv[0][:, j:j + 1])
                    ins.then_inc(h2_scaled, 1)

            def stages(e, n):
                if n == 2:
                    copy_h1(e)
                if n == 4:
                    centre1(e)
                if n == 6:
                    copy_a1(e)
                if n == 7:
                    scale_h2(e)

            act.wait_ge(first_w_landed, 16)
            act.copy(w_hi[:, 0, 0:N1], w_raw[:, 0, 0:N1])
            act.wait_ge(first_x_landed, 16)
            act.copy(x_hi[:, 0, 0:GC], x_raw[:, 0, 0:GC]).then_inc(first_hi, 1)
            act.wait_ge(w_landed[0], 16)
            act.copy(w_hi[:, 0, N1:], w_raw[:, 0, N1:])
            act.wait_ge(x_landed[0], 16)
            act.copy(x_hi[:, 0, GC:], x_raw[:, 0, GC:]).then_inc(hi_ready, 1)
            for s in range(1, RING):
                split_hi(0, 0, s)
            with act.Fori(1, ROUNDS) as r:
                for s in range(RING):
                    split_hi(0, r, s)
            with act.Fori(1, GROUPS) as g:
                for n in range(EPI):
                    split_hi(g, n // RING, n % RING)
                    stages(g - 1, n)
                with act.Fori(EPI // RING, ROUNDS) as r:
                    for s in range(RING):
                        split_hi(g, r, s)
            for n in range(EPI):
                stages(GROUPS - 1, n)

        @block.vector
        def _(dve):
            STEPS = 20
            taken = [0]

            def step(e, ins):
                taken[0] += 1
                ins.then_inc(dve_step, 1)
                dve.wait_ge(dve_step, STEPS * e + taken[0])

            def split_lo(g, r, s):
                u = r * RING + s
                dve.wait_ge(hi_ready, g * UNITS + u + 1)
                dve.tensor_tensor(w_lo[:, s, :], w_raw[:, u, :], w_hi[:, s, :].bitcast(F32), ALU.subtract)
                dve.tensor_tensor(x_lo[:, s, :], x_raw[:, s, :], x_hi[:, s, :].bitcast(F32),
                                  ALU.subtract).then_inc(lo_ready, 1)

            def copy_h1(e):
                dve.wait_ge(multiplied, (e + 1) * UNITS)
                for t in range(T):
                    cols = slice(t * 2 * P, (t + 1) * 2 * P)
                    dve.tensor_copy(h1_fm[:, 1, cols], acc[:, e % 2, 1, cols]).then_inc(h1_copied[t], 1)

            def mean(layer, a, b):
                st = stats[layer]
                return dve.scalar_tensor_tensor(out=neg_mean[layer][:, a:b], in0=st[:, a:b, 1], scalar=-1.0,
                                                in1=st[:, a:b, 4], op0=ALU.mult, op1=ALU.subtract)

            def spread(layer):
                st = stats[layer]
                dve.tensor_tensor(dev[layer][:], st[:, :, 2], st[:, :, 5], ALU.add)
                return dve.tensor_tensor(gap[layer][:], st[:, :, 1], st[:, :, 4], ALU.subtract)

            def square_gap(layer):
                return dve.tensor_tensor(gap[layer][:], gap[layer][:], gap[layer][:], ALU.mult)

            def variance(layer):
                dve.scalar_tensor_tensor(out=var[layer][:], in0=dev[layer][:], scalar=4.0 / (N1, N2, N3)[layer],
                                         in1=gap[layer][:], op0=ALU.mult, op1=ALU.add)\
                    .then_inc(var_ready[layer], 1)

            def leaky(x):
                return dve.scalar_tensor_tensor(out=x, in0=x, scalar=LEAK, in1=x, op0=ALU.mult, op1=ALU.max)

            def statistics1(e):
                for t in range(T):
                    dve.wait_ge(h1_turned, T * e + t + 1)
                    for h in range(2):
                        ins = dve.bn_stats(stats[0][:, 2 * t + h, :], h1_ps[:, t, h, :])
                    step(e, ins)
                    mean(0, 2 * t, 2 * t + 2).then_inc(mean1_ready, 1)
                step(e, spread(0))
                step(e, square_gap(0))
                variance(0)

            def leak1(e):
                for t in range(T):
                    dve.wait_ge(centred1, T * e + t + 1)
                    leaky(a1[:, 2 * t:2 * t + 2, :]).then_inc(a1_ready, 1)

            def copy_a1(e):
                dve.wait_ge(a1_turned, T * (e + 1))
                dve.tensor_copy(a1_fm[:, :, 2 * P:], a1_ps[:, 1]).then_inc(a1_copied[1], 1)

            def layer2(e):
                for t in range(T):
                    dve.wait_ge(h2_scaled, T * e + t + 1)
                    for h in range(2):
                        ins = dve.bn_stats(stats[1][:, 2 * t + h, :], h2[:, 2 * t + h, :])
                    step(e, ins)
                    step(e, mean(1, 2 * t, 2 * t + 2))
                    for j in range(2 * t, 2 * t + 2):
                        ins = dve.tensor_scalar(a2[:, j, :], h2[:, j, :], 2.0, neg_mean[1][:, j:j + 1],
                                                ALU.mult, ALU.add)
                    step(e, ins)
                    leaky(a2[:, 2 * t:2 * t + 2, :]).then_inc(a2_ready, 1)
                step(e, spread(1))
                step(e, square_gap(1))
                variance(1)

            def copy_a2(e):
                for t in range(T):
                    dve.wait_ge(a2_turned, T * e + t + 1)
                    dve.tensor_copy(a2_fm[:, t, :], a2_ps[:, t, :]).then_inc(a2_copied, 1)

            def layer3(e):
                dve.wait_ge(inv_ready[1], e + 1)
                for t in range(T):
                    dve.wait_ge(h3_summed, T * e + t + 1)
                    ins = dve.tensor_scalar(a3[:, t, :], h3_ps[:, t, 0, :], inv[1][:, 2 * t:2 * t + 1], None, ALU.mult)
                step(e, ins)
                for t in range(T):
                    ins = dve.scalar_tensor_tensor(out=h3[:, t, :], in0=h3_ps[:, t, 1, :],
                                                   scalar=inv[1][:, 2 * t + 1:2 * t + 2], in1=a3[:, t, :],
                                                   op0=ALU.mult, op1=ALU.add)
                step(e, ins)
                for t in range(T):
                    ins = dve.bn_stats(stats[2][:, t, :], h3[:, t, :])
                step(e, ins)
                mean(2, 0, T)
                step(e, spread(2))
                for t in range(T):
                    dve.tensor_scalar(a3[:, t, :], h3[:, t, :], 2.0, neg_mean[2][:, t:t + 1], ALU.mult, ALU.add)
                step(e, square_gap(2))
                variance(2)
                step(e, leaky(a3[:, :, :]))
                step(e, dve.tensor_tensor(weighted[:], a3[:], w4_sb[:], ALU.mult))
                step(e, dve.tensor_reduce(y_sum[:], weighted[:], AX.X, ALU.add))
                dve.wait_ge(inv_ready[2], e + 1)
                dve.tensor_tensor(y[:, bass.ds(e * T, T)], y_sum[:], inv[2][:], ALU.mult).then_inc(y_ready, 1)

            def stages(e, n):
                if n == 0:
                    taken[0] = 0
                if n == 2:
                    copy_h1(e)
                if n == 3:
                    statistics1(e)
                if n == 4:
                    leak1(e)
                if n == 6:
                    copy_a1(e)
                if n == 7:
                    layer2(e)
                if n == 9:
                    copy_a2(e)
                if n == 10:
                    layer3(e)
                    assert taken[0] == STEPS, taken[0]

            dve.wait_ge(first_hi, 1)
            dve.tensor_tensor(w_lo[:, 0, 0:N1], w_raw[:, 0, 0:N1], w_hi[:, 0, 0:N1].bitcast(F32), ALU.subtract)
            dve.tensor_tensor(x_lo[:, 0, 0:GC], x_raw[:, 0, 0:GC], x_hi[:, 0, 0:GC].bitcast(F32),
                              ALU.subtract).then_inc(first_lo, 1)
            dve.wait_ge(hi_ready, 1)
            dve.tensor_tensor(w_lo[:, 0, N1:], w_raw[:, 0, N1:], w_hi[:, 0, N1:].bitcast(F32), ALU.subtract)
            dve.tensor_tensor(x_lo[:, 0, GC:], x_raw[:, 0, GC:], x_hi[:, 0, GC:].bitcast(F32),
                              ALU.subtract).then_inc(lo_ready, 1)
            for s in range(1, RING):
                split_lo(0, 0, s)
            with dve.Fori(1, ROUNDS) as r:
                for s in range(RING):
                    split_lo(0, r, s)
            dve.wait_ge(small_landed, 48)
            with dve.Fori(1, GROUPS) as g:
                for n in range(EPI):
                    split_lo(g, n // RING, n % RING)
                    stages(g - 1, n)
                with dve.Fori(EPI // RING, ROUNDS) as r:
                    for s in range(RING):
                        split_lo(g, r, s)
            for n in range(EPI):
                stages(GROUPS - 1, n)

        @block.tensor
        def _(pe):
            def multiply(g, s, chunks, hi, lo, start=False):
                wh = w_hi[:, s, :].rearrange("p (c m n) -> p c m n", c=UC, m=M)
                wl = w_lo[:, s, :].rearrange("p (c m n) -> p c m n", c=UC, m=M)
                xh = x_hi[:, s, :].rearrange("p (c n) -> p c n", c=UC)
                xl = x_lo[:, s, :].rearrange("p (c n) -> p c n", c=UC)
                pe.wait_ge(*hi)
                for c in chunks:
                    for m in range(M):
                        pe.matmul(acc[:, g % 2, m, :], wh[:, c, m, :], xh[:, c, :],
                                  start=(start and c == 0), stop=False, skip_group_check=True)
                pe.wait_ge(*lo)
                for c in chunks:
                    for m in range(M):
                        pe.matmul(acc[:, g % 2, m, :], wh[:, c, m, :], xl[:, c, :],
                                  start=False, stop=False, skip_group_check=True)
                        ins = pe.matmul(acc[:, g % 2, m, :], wl[:, c, m, :], xh[:, c, :],
                                        start=False, stop=True, skip_group_check=True)
                return ins

            def unit(g, r, s, start=False):
                n = g * UNITS + r * RING + s + 1
                multiply(g, s, range(UC), (hi_ready, n), (lo_ready, n), start).then_inc(multiplied, 1)

            def turn_h1(e):
                for t in range(T):
                    pe.wait_ge(h1_copied[t], 2 * (e + 1))
                    for h in range(2):
                        j = 2 * t + h
                        for m in range(M):
                            ins = pe.transpose(h1_ps[:, t, h, m * P:(m + 1) * P],
                                               h1_fm[:, m, j * P:(j + 1) * P], ident[:])
                    ins.then_inc(h1_turned, 1)

            def turn_a1(e):
                for t in range(T):
                    pe.wait_ge(a1_ready, T * e + t + 1)
                    for h in range(2):
                        for m in range(M):
                            ins = pe.transpose(a1_ps[:, t, m, h * P:(h + 1) * P],
                                               a1[:, 2 * t + h, m * P:(m + 1) * P], ident[:])
                    ins.then_inc(a1_turned, 1)

            def layer2(e):
                for t in range(T):
                    pe.wait_ge(a1_copied[t], e + 1)
                    for h in range(2):
                        j = 2 * t + h
                        for m in range(M):
                            ins = pe.matmul(h2_ps[:, t, h, :], a1_fm[:, m, j * P:(j + 1) * P],
                                            w2_sb[:, m, :], start=(m == 0), stop=(m == M - 1))
                    ins.then_inc(h2_summed, 1)

            def turn_a2(e):
                for t in range(T):
                    pe.wait_ge(a2_ready, T * e + t + 1)
                    pe.transpose(a2_ps[:, t, :], a2[:, 2 * t:2 * t + 2, :].rearrange("p h n -> p (h n)"),
                                 ident[:]).then_inc(a2_turned, 1)

            def layer3(e):
                for t in range(T):
                    pe.wait_ge(a2_copied, T * e + t + 1)
                    pe.matmul(h3_ps[:, t].rearrange("p h n -> p (h n)"), a2_fm[:, t, :], w3_sb[:],
                              start=True, stop=True).then_inc(h3_summed, 1)

            def stages(e, n):
                if n == 0:
                    turn_h1(e)
                if n == 3:
                    turn_a1(e)
                if n == 4:
                    layer2(e)
                if n == 7:
                    turn_a2(e)
                if n == 8:
                    layer3(e)

            multiply(0, 0, [0], (first_hi, 1), (first_lo, 1), start=True)
            multiply(0, 0, [1], (hi_ready, 1), (lo_ready, 1)).then_inc(multiplied, 1)
            for s in range(1, RING):
                unit(0, 0, s)
            with pe.Fori(1, ROUNDS) as r:
                for s in range(RING):
                    unit(0, r, s)
            pe.wait_ge(ident_ready, 1)
            pe.wait_ge(small_landed, 48)
            with pe.Fori(1, GROUPS) as g:
                for n in range(EPI):
                    unit(g, n // RING, n % RING, start=(n == 0))
                    stages(g - 1, n)
                with pe.Fori(EPI // RING, ROUNDS) as r:
                    for s in range(RING):
                        unit(g, r, s)
            for n in range(EPI):
                stages(GROUPS - 1, n)


def kernel(r_x, L0_rec_W1, L0_rec_W2, L0_rec_W3, L0_rec_W4):
    import numpy as np
    import concourse.bacc as bacc
    from concourse.bass_utils import run_bass_kernel_spmd

    x = np.asarray(r_x).reshape(P, GROUPS, T, 2, UNITS, UC, P)
    x = np.ascontiguousarray(x.transpose(1, 4, 6, 5, 2, 3, 0)).reshape(GROUPS, UNITS, P, UC * GC)
    w1 = np.asarray(L0_rec_W1).reshape(N1, UNITS, UC, P)
    w1 = np.ascontiguousarray(w1.transpose(1, 3, 2, 0)).reshape(UNITS, P, UC * N1)
    w2 = np.ascontiguousarray(np.asarray(L0_rec_W2).reshape(N2, M, P).transpose(2, 1, 0))
    w3 = np.zeros((2, N2, 2, N3), np.asarray(L0_rec_W3).dtype)
    for h in range(2):
        w3[h, :, h, :] = np.asarray(L0_rec_W3)[:, h * N2:(h + 1) * N2].T
    w3 = w3.reshape(P, 2 * N3)
    w4 = np.ascontiguousarray(np.concatenate([np.asarray(L0_rec_W4)] * T))

    nc = bacc.Bacc("TRN2", target_bir_lowering=False, num_devices=1)
    arrays = {"x": x, "w1": w1, "w2": w2, "w3": w3, "w4": w4}
    args = [nc.dram_tensor(n, a.shape, mybir.dt.from_np(a.dtype), kind="ExternalInput").ap() for n, a in arrays.items()]
    out = nc.dram_tensor("out", (P, TILES), F32, kind="ExternalOutput").ap()
    rec_kernel(nc, *args, out)
    r = run_bass_kernel_spmd(nc, [arrays], core_ids=[0])
    return np.asarray(r.results[0]["out"]).reshape(ROWS, 1)
```

```python
from contextlib import ExitStack

import concourse.bass as bass
from concourse import mybir

ALU = mybir.AluOpType
ACT = mybir.ActivationFunctionType
AX = mybir.AxisListType
F32 = mybir.dt.float32
F32R = mybir.dt.float32r

P = 128
F = 5120
N1, N2, N3 = 256, 64, 8
ROWS = 1024
CHUNKS = F // P
UC = 2
UNITS = CHUNKS // UC
RING = 4
ROUNDS = UNITS // RING
GR = 256
GROUPS = ROWS // GR
T = GR // P
GC = 2 * GR
TILES = ROWS // P
M = N1 // P
J = 2 * T
LEAK = 0.05
WARM_UP = 8
EPI = 8


def is_first(n):
    return isinstance(n, int) and n == 0


def rec_kernel(nc, x, w1, w2, w3, w4, out):
    with ExitStack() as ctx:
        def sb(name, shape, dt=F32):
            return ctx.enter_context(nc.sbuf_tensor(name, shape, dt))

        def ps(name, shape):
            return ctx.enter_context(nc.psum_tensor(name, shape, F32))

        def sem(name):
            return ctx.enter_context(nc.semaphore(name))

        x_raw = sb("x_raw", [P, RING, UC * GC])
        x_hi = sb("x_hi", [P, RING, UC * GC], F32R)
        x_lo = sb("x_lo", [P, RING, UC * GC], F32R)
        w_raw = sb("w_raw", [P, UNITS, UC * N1])
        w_mean = sb("w_mean", [P, UNITS, UC])
        w_sum = sb("w_sum", [P, RING])
        unused = sb("unused", [P, N1])
        w_hi = sb("w_hi", [P, RING, UC * N1], F32R)
        w_lo = sb("w_lo", [P, RING, UC * N1], F32R)
        w2_raw = sb("w2_raw", [P, M, N2])
        w2_sb = sb("w2_sb", [P, 2, M, 2 * N2])
        w3_sb = sb("w3_sb", [P, 2 * N3])
        w2_mean = sb("w2_mean", [P, M])
        w3_mean = sb("w3_mean", [P, 2])
        w4_sb = sb("w4_sb", [P, T, N3])
        ones = sb("ones", [P, 1])
        half_ones = sb("half_ones", [P, 2])
        zeros = sb("zeros", [P, GC], mybir.dt.bfloat16)
        h1_fm = sb("h1_fm", [P, M, GC])
        a1_fm = sb("a1_fm", [P, M, GC])
        sq1_fm = sb("sq1_fm", [P, M, GC])
        sq1_sum = sb("sq1_sum", [P, GC])
        h2_fm = sb("h2_fm", [P, T, P])
        a2_fm = sb("a2_fm", [P, T, P])
        sq2_fm = sb("sq2_fm", [P, T, P])
        half3 = sb("half3", [P, T, 2, N3])
        h3 = sb("h3", [P, T, N3])
        a3 = sb("a3", [P, T, N3])
        weighted = sb("weighted", [P, T, N3])
        y_sum = sb("y_sum", [P, T])
        y = sb("y", [P, TILES])
        sq3 = sb("sq3", [P, T, N3])
        var1 = sb("var1", [P, J])
        var2 = sb("var2", [P, J])
        var12 = sb("var12", [P, J])
        inv12 = sb("inv12", [P, J])
        var3 = sb("var3", [P, T])
        inv3 = sb("inv3", [P, T])
        var1_inverse = sb("var1_inverse", [P, J])
        minus_half = sb("minus_half", [P, J])

        acc = ps("acc", [P, 2, M, GC])
        h2_ps = ps("h2_ps", [P, T, GC])
        h3_bank = ps("h3_bank", [P, GC])
        var2_bank = ps("var2_bank", [P, GC])
        h3_ps = h3_bank[:, 0:T * 2 * N3].rearrange("p (t h n) -> p t h n", t=T, h=2)
        var1_ps = h3_bank[:, T * 2 * N3:T * 2 * N3 + J]
        var2_ps = var2_bank[:, 0:J]

        x_landed = [sem(f"x_landed{s}") for s in range(RING)]
        w_landed = [sem(f"w_landed{s}") for s in range(RING)]
        first_w_landed = sem("first_w_landed")
        first_x_landed = sem("first_x_landed")
        small_landed = sem("small_landed")
        w_mean_step = sem("w_mean_step")
        w23_centred = sem("w23_centred")
        zeros_ready = sem("zeros_ready")
        w2_zeroed = sem("w2_zeroed")
        half_ready = sem("half_ready")
        ones_ready = sem("ones_ready")
        first_mean = sem("first_mean")
        first_sum = sem("first_sum")
        w_summed = sem("w_summed")
        mean_a_ready = sem("mean_a_ready")
        mean_b_ready = sem("mean_b_ready")
        first_hi = sem("first_hi")
        first_lo = sem("first_lo")
        first_w_hi = sem("first_w_hi")
        hi_ready = sem("hi_ready")
        lo_ready = sem("lo_ready")
        multiplied = sem("multiplied")
        block0_multiplied = sem("block0_multiplied")
        h1_copied = sem("h1_copied")
        h1_squared = sem("h1_squared")
        a1_ready = sem("a1_ready")
        sq1_summed = sem("sq1_summed")
        h2_summed = sem("h2_summed")
        h2_copied = sem("h2_copied")
        h2_squared = sem("h2_squared")
        a2_ready = sem("a2_ready")
        h3_summed = sem("h3_summed")
        var1_summed = sem("var1_summed")
        var1_copied = sem("var1_copied")
        var1_inverted = sem("var1_inverted")
        var2_summed = sem("var2_summed")
        var2_ready = sem("var2_ready")
        var12_ready = sem("var12_ready")
        inv12_ready = sem("inv12_ready")
        var3_ready = sem("var3_ready")
        inv3_ready = sem("inv3_ready")
        y_ready = sem("y_ready")
        dve_step = sem("dve_step")
        y_stored = sem("y_stored")

        H1_PARTS = [(0, 0, GC)] + [(1, t * 2 * P, (t + 1) * 2 * P) for t in range(T)]
        PARTS = len(H1_PARTS)

        block = ctx.enter_context(nc.Block())

        @block.sync
        def _(sp):
            def load(g, r, s, first=False):
                u = r * RING + s
                if not first:
                    sp.wait_ge(lo_ready, g * UNITS + (r - 1) * RING + s + 1)
                if is_first(g):
                    sp.dma_start(w_raw[:, bass.ds(u, 1), :],
                                 w1[bass.ds(u, 1)].rearrange("a p n -> p a n")).then_inc(w_landed[s], 16)
                sp.dma_start(x_raw[:, s, :],
                             x[g, bass.ds(u, 1)].rearrange("a p n -> p (a n)")).then_inc(x_landed[s], 16)

            sp.dma_start(w_raw[:, 0, 0:N1], w1[0, :, 0:N1]).then_inc(first_w_landed, 16)
            sp.dma_start(x_raw[:, 0, 0:GC], x[0, 0, :, 0:GC]).then_inc(first_x_landed, 16)
            sp.dma_start(w_raw[:, 0, N1:], w1[0, :, N1:]).then_inc(w_landed[0], 16)
            sp.dma_start(x_raw[:, 0, GC:], x[0, 0, :, GC:]).then_inc(x_landed[0], 16)
            for s in range(1, RING):
                load(0, 0, s, first=True)
            with sp.Fori(1, ROUNDS) as r:
                for s in range(RING):
                    load(0, r, s)
            sp.dma_start(w2_raw[:], w2).then_inc(small_landed, 16)
            sp.dma_start(w3_sb[:], w3).then_inc(small_landed, 16)
            sp.dma_start(w4_sb[:], w4.rearrange("(o t) n -> o t n", o=1).broadcast_to([P, T, N3]))\
                .then_inc(small_landed, 16)
            with sp.Fori(1, GROUPS) as g:
                with sp.Fori(0, ROUNDS) as r:
                    for s in range(RING):
                        load(g, r, s)
            sp.wait_ge(y_ready, GROUPS)
            sp.dma_start(out, y[:]).then_inc(y_stored, 16)
            sp.wait_ge(y_stored, 16)

        @block.gpsimd
        def _(pool):
            pool.memset(zeros[:], 0.0).then_inc(zeros_ready, 1)
            pool.memset(w2_sb[:], 0.0).then_inc(w2_zeroed, 1)
            pool.memset(minus_half[:], -0.5).then_inc(half_ready, 1)
            pool.memset(half_ones[:], 0.0).then_inc(half_ready, 1)
            pool.memset(ones[:], 1.0).then_inc(ones_ready, 1)
            pool.wait_ge(half_ready, 2)
            for h in range(2):
                pool.wait_ge(ones_ready, h + 1)
                pool.memset(half_ones[h * N2:(h + 1) * N2, h:h + 1], 1.0).then_inc(ones_ready, 1)

            with pool.Fori(0, GROUPS) as e:
                pool.wait_ge(var12_ready, e + 1)
                pool.tensor_tensor(inv12[:], var12[:], minus_half[:], ALU.pow).then_inc(inv12_ready, 1)
                pool.wait_ge(var3_ready, e + 1)
                pool.tensor_tensor(inv3[:], var3[:], minus_half[:, 0:T], ALU.pow).then_inc(inv3_ready, 1)

        @block.scalar
        def _(act):
            def centre_w(u, s, c):
                return act.activation(w_hi[:, s, c * N1:(c + 1) * N1], w_raw[:, u, c * N1:(c + 1) * N1],
                                      ACT.Identity, bias=w_mean[:, u, c:c + 1], scale=1.0)

            def split_hi(g, r, s):
                u = r * RING + s
                if is_first(g):
                    act.wait_ge(w_landed[s], 16 * (r + 1))
                    act.activation(unused[:], w_raw[:, u, N1:], ACT.Copy, scale=-1.0 / N1,
                                   accum_out=w_mean[:, u, 1:2]).then_inc(mean_b_ready, 1)
                if is_first(g) and is_first(r):
                    act.wait_ge(mean_a_ready, u)
                    act.wait_ge(mean_b_ready, u)
                    centre_w(u, s, 0)
                    centre_w(u, s, 1).then_inc(first_w_hi, 1)
                    act.wait_ge(x_landed[s], 16)
                    act.copy(x_hi[:, s, :], x_raw[:, s, :]).then_inc(hi_ready, 1)
                    return
                act.wait_ge(x_landed[s], 16 * (g * ROUNDS + r + 1))
                act.wait_ge(multiplied, g * UNITS + (r - 1) * RING + s + 1)
                act.copy(x_hi[:, s, :], x_raw[:, s, :])
                if is_first(g):
                    act.wait_ge(mean_a_ready, u)
                    act.wait_ge(mean_b_ready, u)
                centre_w(u, s, 0)
                centre_w(u, s, 1).then_inc(hi_ready, 1)

            def copy_h1(e, parts):
                for k in parts:
                    if k == 0:
                        act.wait_ge(block0_multiplied, e + 1)
                    else:
                        act.wait_ge(multiplied, (e + 1) * UNITS)
                    m, a, b = H1_PARTS[k]
                    act.copy(h1_fm[:, m, a:b], acc[:, e % 2, m, a:b]).then_inc(h1_copied, 1)

            def square_h1(e, parts):
                for k in parts:
                    act.wait_ge(h1_copied, PARTS * e + k + 1)
                    m, a, b = H1_PARTS[k]
                    act.activation(sq1_fm[:, m, a:b], h1_fm[:, m, a:b], ACT.Square, scale=N1 ** -0.5)\
                        .then_inc(h1_squared, 1)

            def copy_h2(e):
                for t in range(T):
                    act.wait_ge(h2_summed, T * e + t + 1)
                    act.copy(h2_fm[:, t, :], h2_ps[:, t, 0:P]).then_inc(h2_copied, 1)
                    act.activation(sq2_fm[:, t, :], h2_ps[:, t, 0:P], ACT.Square, scale=N2 ** -0.5)\
                        .then_inc(h2_squared, 1)

            def stages(e, n):
                if n == 1:
                    copy_h1(e, [0])
                    square_h1(e, [0])
                    copy_h1(e, range(1, PARTS))
                    square_h1(e, range(1, PARTS))
                if n == 3:
                    copy_h2(e)

            act.wait_ge(first_mean, 1)
            centre_w(0, 0, 0)
            act.wait_ge(first_x_landed, 16)
            act.copy(x_hi[:, 0, 0:GC], x_raw[:, 0, 0:GC]).then_inc(first_hi, 1)
            act.wait_ge(first_mean, 2)
            centre_w(0, 0, 1)
            act.wait_ge(x_landed[0], 16)
            act.copy(x_hi[:, 0, GC:], x_raw[:, 0, GC:]).then_inc(hi_ready, 1)
            for s in range(1, RING):
                split_hi(0, 0, s)
            with act.Fori(1, ROUNDS) as r:
                for s in range(RING):
                    split_hi(0, r, s)
            with act.Fori(1, GROUPS) as g:
                for n in range(EPI):
                    split_hi(g, n // RING, n % RING)
                    stages(g - 1, n)
                with act.Fori(EPI // RING, ROUNDS) as r:
                    for s in range(RING):
                        split_hi(g, r, s)
            for n in range(EPI):
                stages(GROUPS - 1, n)

        @block.vector
        def _(dve):
            STEPS = 6
            taken = [0]

            def step(e, ins):
                taken[0] += 1
                ins.then_inc(dve_step, 1)
                dve.wait_ge(dve_step, STEPS * e + taken[0])

            def low_w(u, s, c):
                cols = slice(c * N1, (c + 1) * N1)
                return dve.scalar_tensor_tensor(out=w_lo[:, s, cols], in0=w_raw[:, u, cols],
                                                scalar=w_mean[:, u, c:c + 1], in1=w_hi[:, s, cols].bitcast(F32),
                                                op0=ALU.add, op1=ALU.subtract)

            def split_lo(g, r, s, next_unit=None):
                u = r * RING + s
                if next_unit:
                    r1, s1 = next_unit
                    u1 = r1 * RING + s1
                    dve.wait_ge(w_landed[s1], 16 * (r1 + 1))
                    dve.tensor_reduce(w_sum[:, s1:s1 + 1], w_raw[:, u1, 0:N1], AX.X, ALU.add).then_inc(w_summed, 1)
                if is_first(g) and is_first(r):
                    dve.wait_ge(first_w_hi, s)
                else:
                    dve.wait_ge(hi_ready, g * UNITS + u + 1)
                low_w(u, s, 0)
                low_w(u, s, 1)
                if next_unit:
                    dve.wait_ge(w_summed, u1)
                    dve.tensor_scalar(w_mean[:, u1, 0:1], w_sum[:, s1:s1 + 1], -1.0 / N1, None, ALU.mult)\
                        .then_inc(mean_a_ready, 1)
                if is_first(g) and is_first(r):
                    dve.wait_ge(hi_ready, u + 1)
                dve.tensor_tensor(x_lo[:, s, :], x_raw[:, s, :], x_hi[:, s, :].bitcast(F32),
                                  ALU.subtract).then_inc(lo_ready, 1)

            def leaky(out, x):
                return dve.scalar_tensor_tensor(out=out, in0=x, scalar=LEAK, in1=x, op0=ALU.mult, op1=ALU.max)

            def leak1(e):
                for k, (m, a, b) in enumerate(H1_PARTS):
                    dve.wait_ge(h1_copied, PARTS * e + k + 1)
                    leaky(a1_fm[:, m, a:b], h1_fm[:, m, a:b]).then_inc(a1_ready, 1)

            def sum_squares1(e):
                for k in range(1, PARTS):
                    dve.wait_ge(h1_squared, PARTS * e + k + 1)
                    _, a, b = H1_PARTS[k]
                    dve.tensor_tensor(sq1_sum[:, a:b], sq1_fm[:, 0, a:b], sq1_fm[:, 1, a:b], ALU.add)\
                        .then_inc(sq1_summed, 1)

            def variance1(e):
                dve.wait_ge(var1_summed, e + 1)
                dve.reciprocal(var1_inverse[:], var1_ps).then_inc(var1_inverted, 1)
                dve.tensor_copy(var1[:], var1_ps).then_inc(var1_copied, 1)

            def leak2(e):
                for t in range(T):
                    dve.wait_ge(h2_copied, T * e + t + 1)
                    leaky(a2_fm[:, t, :], h2_fm[:, t, :]).then_inc(a2_ready, 1)

            def variance2(e):
                dve.wait_ge(var2_summed, e + 1)
                dve.wait_ge(var1_inverted, e + 1)
                dve.tensor_tensor(var2[:], var2_ps, var1_inverse[:], ALU.mult).then_inc(var2_ready, 1)
                dve.wait_ge(var2_ready, e + 1)
                dve.wait_ge(var1_copied, e + 1)
                dve.tensor_tensor(var12[:], var2[:], var1[:], ALU.mult).then_inc(var12_ready, 1)

            def layer3(e):
                dve.wait_ge(inv12_ready, e + 1)
                dve.wait_ge(h3_summed, e + 1)
                each_inv12 = inv12[:].rearrange("p (t h o) -> p t h o", h=2, o=1).broadcast_to([P, T, 2, N3])
                step(e, dve.tensor_tensor(half3[:], h3_ps, each_inv12, ALU.mult))
                step(e, dve.tensor_tensor(h3[:], half3[:, :, 0, :], half3[:, :, 1, :], ALU.add))
                step(e, dve.scalar_tensor_tensor(out=sq3[:], in0=h3[:], scalar=1.0 / N3, in1=h3[:],
                                                 op0=ALU.mult, op1=ALU.mult))
                dve.tensor_reduce(var3[:], sq3[:], AX.X, ALU.add).then_inc(var3_ready, 1)
                step(e, leaky(a3[:], h3[:]))
                step(e, dve.tensor_tensor(weighted[:], a3[:], w4_sb[:], ALU.mult))
                step(e, dve.tensor_reduce(y_sum[:], weighted[:], AX.X, ALU.add))
                dve.wait_ge(inv3_ready, e + 1)
                dve.tensor_tensor(y[:, bass.ds(e * T, T)], y_sum[:], inv3[:], ALU.mult).then_inc(y_ready, 1)

            def stages(e, n):
                if n == 0:
                    taken[0] = 0
                if n == 1:
                    leak1(e)
                    sum_squares1(e)
                if n == 4:
                    leak2(e)
                    variance1(e)
                if n == 5:
                    variance2(e)
                if n == 7:
                    layer3(e)
                    assert taken[0] == STEPS, taken[0]

            for c, landed in ((0, first_w_landed), (1, w_landed[0])):
                dve.wait_ge(landed, 16)
                dve.tensor_reduce(w_sum[:, c:c + 1], w_raw[:, 0, c * N1:(c + 1) * N1], AX.X, ALU.add)\
                    .then_inc(first_sum, 1)
                dve.wait_ge(first_sum, c + 1)
                dve.tensor_scalar(w_mean[:, 0, c:c + 1], w_sum[:, c:c + 1], -1.0 / N1, None, ALU.mult)\
                    .then_inc(first_mean, 1)
            dve.wait_ge(first_mean, 2)
            dve.wait_ge(first_hi, 1)
            low_w(0, 0, 0)
            dve.tensor_tensor(x_lo[:, 0, 0:GC], x_raw[:, 0, 0:GC], x_hi[:, 0, 0:GC].bitcast(F32),
                              ALU.subtract).then_inc(first_lo, 1)
            dve.wait_ge(w_landed[1], 16)
            dve.tensor_reduce(w_sum[:, 1:2], w_raw[:, 1, 0:N1], AX.X, ALU.add).then_inc(w_summed, 1)
            dve.wait_ge(hi_ready, 1)
            low_w(0, 0, 1)
            dve.wait_ge(w_summed, 1)
            dve.tensor_scalar(w_mean[:, 1, 0:1], w_sum[:, 1:2], -1.0 / N1, None, ALU.mult).then_inc(mean_a_ready, 1)
            dve.tensor_tensor(x_lo[:, 0, GC:], x_raw[:, 0, GC:], x_hi[:, 0, GC:].bitcast(F32),
                              ALU.subtract).then_inc(lo_ready, 1)
            for s in range(1, RING):
                split_lo(0, 0, s, ((s + 1) // RING, (s + 1) % RING))
            with dve.Fori(1, ROUNDS - 1) as r:
                for s in range(RING):
                    split_lo(0, r, s, (r + (s + 1) // RING, (s + 1) % RING))
            for s in range(RING):
                split_lo(0, ROUNDS - 1, s, (ROUNDS - 1, s + 1) if s + 1 < RING else None)
            dve.wait_ge(small_landed, 48)
            dve.wait_ge(w2_zeroed, 1)
            w3_blocks = w3_sb[:].rearrange("p (h n) -> p h n", h=2)
            dve.tensor_reduce(w2_mean[:], w2_raw[:], AX.X, ALU.add)
            dve.tensor_reduce(w3_mean[:], w3_blocks, AX.X, ALU.add).then_inc(w_mean_step, 1)
            dve.wait_ge(w_mean_step, 1)
            dve.tensor_scalar(w2_mean[:], w2_mean[:], 1.0 / N2, None, ALU.mult)
            dve.tensor_scalar(w3_mean[:], w3_mean[:], 1.0 / N3, None, ALU.mult).then_inc(w_mean_step, 1)
            dve.wait_ge(w_mean_step, 2)
            for h in range(2):
                for m in range(M):
                    dve.tensor_scalar(w2_sb[:, h, m, h * N2:(h + 1) * N2], w2_raw[:, m, :], w2_mean[:, m:m + 1],
                                      None, ALU.subtract)
            for k in range(2):
                ins = dve.tensor_scalar(w3_blocks[:, k, :], w3_blocks[:, k, :], w3_mean[:, k:k + 1], None,
                                        ALU.subtract)
            ins.then_inc(w23_centred, 1)
            with dve.Fori(1, GROUPS) as g:
                for n in range(EPI):
                    split_lo(g, n // RING, n % RING)
                    stages(g - 1, n)
                with dve.Fori(EPI // RING, ROUNDS) as r:
                    for s in range(RING):
                        split_lo(g, r, s)
            for n in range(EPI):
                stages(GROUPS - 1, n)

        @block.tensor
        def _(pe):
            def multiply(g, s, chunks, hi, lo, blocks=range(M), start=False):
                wh = w_hi[:, s, :].rearrange("p (c m n) -> p c m n", c=UC, m=M)
                wl = w_lo[:, s, :].rearrange("p (c m n) -> p c m n", c=UC, m=M)
                xh = x_hi[:, s, :].rearrange("p (c n) -> p c n", c=UC)
                xl = x_lo[:, s, :].rearrange("p (c n) -> p c n", c=UC)
                pe.wait_ge(*hi)
                for c in chunks:
                    for m in blocks:
                        pe.matmul(acc[:, g % 2, m, :], wh[:, c, m, :], xh[:, c, :],
                                  start=(start and c == 0), stop=False, skip_group_check=True)
                pe.wait_ge(*lo)
                for c in chunks:
                    for m in blocks:
                        pe.matmul(acc[:, g % 2, m, :], wh[:, c, m, :], xl[:, c, :],
                                  start=False, stop=False, skip_group_check=True)
                        ins = pe.matmul(acc[:, g % 2, m, :], wl[:, c, m, :], xh[:, c, :],
                                        start=False, stop=True, skip_group_check=True)
                return ins

            def parts_ready(g, r, s):
                n = g * UNITS + r * RING + s + 1
                return (hi_ready, n), (lo_ready, n)

            def unit(g, r, s, start=False):
                multiply(g, s, range(UC), *parts_ready(g, r, s), start=start).then_inc(multiplied, 1)

            def last_round(g):
                r = ROUNDS - 1
                for s in range(RING - 2):
                    unit(g, r, s)
                for s in (RING - 2, RING - 1):
                    ins = multiply(g, s, range(UC), *parts_ready(g, r, s), blocks=[0])
                ins.then_inc(block0_multiplied, 1)
                for s in (RING - 2, RING - 1):
                    multiply(g, s, range(UC), *parts_ready(g, r, s), blocks=[1]).then_inc(multiplied, 1)

            def layer2(e):
                def add(t, m):
                    for h in range(2):
                        j = 2 * t + h
                        ins = pe.matmul(h2_ps[:, t, 0:P], w2_sb[:, h, m, :], a1_fm[:, m, j * P:(j + 1) * P],
                                        start=(h == 0 and m == 0), stop=(h == 1 and m == M - 1))
                    return ins

                pe.wait_ge(a1_ready, PARTS * e + 1)
                for t in range(T):
                    add(t, 0)
                for t in range(T):
                    pe.wait_ge(a1_ready, PARTS * e + t + 2)
                    add(t, 1).then_inc(h2_summed, 1)

            def sum_variance1(e):
                for t in range(T):
                    pe.wait_ge(sq1_summed, T * e + t + 1)
                    for j in range(2 * t, 2 * t + 2):
                        ins = pe.matmul(var1_ps[:, j:j + 1], sq1_sum[:, j * P:(j + 1) * P], ones[:],
                                        start=True, stop=True)
                ins.then_inc(var1_summed, 1)

            def sum_variance2(e):
                for t in range(T):
                    pe.wait_ge(h2_squared, T * e + t + 1)
                    ins = pe.matmul(var2_ps[:, 2 * t:2 * t + 2], sq2_fm[:, t, :], half_ones[:],
                                    start=True, stop=True)
                ins.then_inc(var2_summed, 1)

            def layer3(e):
                pe.wait_ge(var1_copied, e + 1)
                for t in range(T):
                    pe.wait_ge(a2_ready, T * e + t + 1)
                    ins = pe.matmul(h3_ps[:, t].rearrange("p h n -> p (h n)"), a2_fm[:, t, :], w3_sb[:],
                                    start=True, stop=True)
                ins.then_inc(h3_summed, 1)

            def stages(e, n):
                if n == 1:
                    layer2(e)
                    sum_variance1(e)
                if n == 4:
                    sum_variance2(e)
                    layer3(e)

            pe.wait_ge(zeros_ready, 1)
            for _ in range(WARM_UP):
                pe.matmul(h2_ps[:, 0, :], zeros[:, 0:P], zeros[:], start=True, stop=True)
            multiply(0, 0, [0], (first_hi, 1), (first_lo, 1), start=True)
            multiply(0, 0, [1], (hi_ready, 1), (lo_ready, 1)).then_inc(multiplied, 1)
            for s in range(1, RING):
                unit(0, 0, s)
            with pe.Fori(1, ROUNDS - 1) as r:
                for s in range(RING):
                    unit(0, r, s)
            last_round(0)
            pe.wait_ge(ones_ready, 3)
            pe.wait_ge(w23_centred, 1)
            with pe.Fori(1, GROUPS) as g:
                for n in range(EPI):
                    unit(g, n // RING, n % RING, start=(n == 0))
                    stages(g - 1, n)
                with pe.Fori(EPI // RING, ROUNDS - 1) as r:
                    for s in range(RING):
                        unit(g, r, s)
                last_round(g)
            for n in range(EPI):
                stages(GROUPS - 1, n)


def kernel(r_x, L0_rec_W1, L0_rec_W2, L0_rec_W3, L0_rec_W4):
    import numpy as np
    import concourse.bacc as bacc
    from concourse.bass_utils import run_bass_kernel_spmd

    x = np.asarray(r_x).reshape(P, GROUPS, T, 2, UNITS, UC, P)
    x = np.ascontiguousarray(x.transpose(1, 4, 6, 5, 2, 3, 0)).reshape(GROUPS, UNITS, P, UC * GC)
    w1 = np.asarray(L0_rec_W1).reshape(N1, UNITS, UC, P)
    w1 = np.ascontiguousarray(w1.transpose(1, 3, 2, 0)).reshape(UNITS, P, UC * N1)
    w2 = np.ascontiguousarray(np.asarray(L0_rec_W2).reshape(N2, M, P).transpose(2, 1, 0))
    w3 = np.zeros((2, N2, 2, N3), np.asarray(L0_rec_W3).dtype)
    for h in range(2):
        w3[h, :, h, :] = np.asarray(L0_rec_W3)[:, h * N2:(h + 1) * N2].T
    w3 = w3.reshape(P, 2 * N3)
    w4 = np.ascontiguousarray(np.concatenate([np.asarray(L0_rec_W4)] * T))

    nc = bacc.Bacc("TRN2", target_bir_lowering=False, num_devices=1)
    arrays = {"x": x, "w1": w1, "w2": w2, "w3": w3, "w4": w4}
    args = [nc.dram_tensor(n, a.shape, mybir.dt.from_np(a.dtype), kind="ExternalInput").ap() for n, a in arrays.items()]
    out = nc.dram_tensor("out", (P, TILES), F32, kind="ExternalOutput").ap()
    rec_kernel(nc, *args, out)
    r = run_bass_kernel_spmd(nc, [arrays], core_ids=[0])
    return np.asarray(r.results[0]["out"]).reshape(ROWS, 1)
```
